# Optimizing a Trainium2 kernel written in Bass

```python
import numpy as np
import jax
import jax.numpy as jnp

def _softmax(x, axis=-1):
    return jax.nn.softmax(x, axis=axis)

def _gelu(x):
    return jax.nn.gelu(x, approximate=True)

def _silu(x):
    return jax.nn.silu(x)

def _sigmoid(x):
    return jax.nn.sigmoid(x)

def _layernorm(x, axis=-1, eps=1e-05):
    m = jnp.mean(x, axis=axis, keepdims=True)
    v = jnp.var(x, axis=axis, keepdims=True)
    return (x - m) / jnp.sqrt(v + eps)

def _scatter_add(tgt, idx, src, axis=0):
    return tgt.at[idx].add(src)

def _segment_sum(src, seg, n):
    return jax.ops.segment_sum(src, seg, n)
kernel_name = 'mk_adj_preln_d1_adj_r2_e95156'

def setup_inputs(seed: int=0):
    np.random.seed(seed)
    _w = jnp.asarray

    def _rec_inputs():
        import jax
        import jax.numpy as jnp
        _gk = jax.random.key(seed)
        x = -0.0005207 + 1.001 * jax.random.normal(jax.random.fold_in(_gk, 1), (4096, 128), jnp.float32)
        _w = (1.0 + jnp.arange(4096, dtype=jnp.float32)) ** (-0.5)
        _w = _w / _w.mean()
        _pij = jnp.clip(0.000488281 * _w[:, None] * _w[None, :], 0.0, 1.0)
        _a = jax.random.uniform(jax.random.fold_in(_gk, 2), (4096, 4096)) < _pij
        _a = jnp.logical_or(_a, jnp.eye(4096, dtype=bool))
        _af = _a.astype(jnp.float32)
        _af = _af * jax.random.uniform(jax.random.fold_in(_gk, 3), (4096, 4096), jnp.float32, 0.05, 1)
        adj = _af
        return (x, adj)
    x, adj = _rec_inputs()

    def _L0_gnn_setup():
        import jax, jax.numpy as jnp
        import numpy as np
        N = 4096
        D = 128
        L = 3

        def _cxin_conv(x, a, eps, W, b):
            ax = a @ x
            h = ax + (1.0 + eps[0]) * ax
            for i in range(L):
                h = jax.nn.relu(h @ W[i].T + b[i])
            return h
        key = jax.random.key(seed)
        ks = jax.random.split(key, 8)
        s = 1.0 / np.sqrt(D)
        return {'x1': jax.random.normal(ks[0], (N, D), jnp.float32), 'x2': jax.random.normal(ks[1], (N, D), jnp.float32), 'G1': jax.random.uniform(ks[2], (N, N), jnp.float32), 'G2': jax.random.uniform(ks[3], (N, N), jnp.float32), 'eps1': jnp.zeros((1,), jnp.float32), 'eps2': jnp.zeros((1,), jnp.float32), 'W1': jax.random.normal(ks[4], (L, D, D), jnp.float32) * s, 'b1': jnp.zeros((L, D), jnp.float32), 'W2': jax.random.normal(ks[5], (L, D, D), jnp.float32) * s, 'b2': jnp.zeros((L, D), jnp.float32), 'Wm': jax.random.normal(ks[6], (D, 2 * D), jnp.float32) * (1.0 / np.sqrt(2 * D)), 'bm': jnp.zeros((D,), jnp.float32)}
    _L0_gnn_all = _L0_gnn_setup()
    _L0_gnn_in = {k: v for k, v in _L0_gnn_all.items() if k in ('x2', 'eps1', 'eps2', 'W1', 'b1', 'W2', 'b2', 'Wm', 'bm')}
    del _L0_gnn_all
    return {'x': x, 'adj': adj, 'L0_gnn_x2': _L0_gnn_in['x2'], 'L0_gnn_eps1': _L0_gnn_in['eps1'], 'L0_gnn_eps2': _L0_gnn_in['eps2'], 'L0_gnn_W1': _L0_gnn_in['W1'], 'L0_gnn_b1': _L0_gnn_in['b1'], 'L0_gnn_W2': _L0_gnn_in['W2'], 'L0_gnn_b2': _L0_gnn_in['b2'], 'L0_gnn_Wm': _L0_gnn_in['Wm'], 'L0_gnn_bm': _L0_gnn_in['bm']}

def reference(x, adj, L0_gnn_x2, L0_gnn_eps1, L0_gnn_eps2, L0_gnn_W1, L0_gnn_b1, L0_gnn_W2, L0_gnn_b2, L0_gnn_Wm, L0_gnn_bm):
    import jax
    import jax.numpy as jnp

    def _L0_gnn_ref(x1, x2, G1, G2, eps1, eps2, W1, b1, W2, b2, Wm, bm):
        import jax, jax.numpy as jnp
        import numpy as np
        N = 4096
        D = 128
        L = 3

        def _cxin_conv(x, a, eps, W, b):
            ax = a @ x
            h = ax + (1.0 + eps[0]) * ax
            for i in range(L):
                h = jax.nn.relu(h @ W[i].T + b[i])
            return h
        out1 = _cxin_conv(x1, G1, eps1, W1, b1)
        out2 = _cxin_conv(x2, G2, eps2, W2, b2)
        merged = jnp.concatenate((out1, out2), axis=1)
        return merged @ Wm.T + bm
    h = jnp.maximum(_layernorm(x, axis=-1), 0.0)
    x = x + _L0_gnn_ref(h, L0_gnn_x2, adj, adj, L0_gnn_eps1, L0_gnn_eps2, L0_gnn_W1, L0_gnn_b1, L0_gnn_W2, L0_gnn_b2, L0_gnn_Wm, L0_gnn_bm)
    return x

_drawn_inputs = setup_inputs


def setup_inputs(seed=0):
    import zlib

    import numpy as np

    out = dict(_drawn_inputs(seed))
    spreads = {'L0_gnn_b1': (0.0, 0.1), 'L0_gnn_b2': (0.0, 0.1), 'L0_gnn_bm': (0.0, 0.1)}
    factors = {}
    for name, (base, spread) in spreads.items():
        noise = np.random.default_rng([zlib.crc32(name.encode()), seed]).standard_normal(out[name].shape)
        drawn = base * np.exp(spread * noise) if base else spread * noise
        out[name] = jnp.asarray(drawn.astype(out[name].dtype))
    for name, factor in factors.items():
        out[name] = (out[name] * factor).astype(out[name].dtype)
    return out
```

```python
from contextlib import ExitStack

import concourse.bass as bass
from concourse import mybir


def gnn_layer_kernel(nc, adj_tiles, x_tiles, x2_tiles, x_t, w1_t, w2_t, wm_t, b1_t, b2_t, bm_t, eps1, eps2, out_t):
    F32 = mybir.dt.float32
    F32R = mybir.dt.float32r
    ALU = mybir.AluOpType
    ACT = mybir.ActivationFunctionType

    UNITS_ALL, P, UNIT_COLS = adj_tiles.shape
    D = x_t.shape[0]
    N = x_t.shape[1]
    CW = 512
    JB = UNIT_COLS // CW
    CHUNKS = N // CW
    U = UNITS_ALL // CHUNKS
    BLOCKS = N // P
    RING = 4
    LAYERS = 3
    STEPS = LAYERS + 1
    LN_EPS = 1e-5
    BRANCH_ORDER = (1, 0)
    FIRST_BRANCH = BRANCH_ORDER[0]
    assert U % RING == 0 and U == 8

    LAYER_AFTER = {1: 0, 3: 1, 5: 2}
    MERGE_AFTER = 6
    OPERAND_AFTER = {1: 0, 3: 1, 5: 2, 7: 3}

    with ExitStack() as ctx:
        def sb(name, shape, dt=F32):
            return ctx.enter_context(nc.sbuf_tensor(name, shape, dt))

        def bank(name):
            return ctx.enter_context(nc.psum_tensor(name, [P, CW], F32))

        def sem(name):
            return ctx.enter_context(nc.semaphore(name))

        adj_raw = sb("adj_raw", [P, RING, UNIT_COLS])
        adj_hi = sb("adj_hi", [P, RING, UNIT_COLS], F32R)
        adj_lo = sb("adj_lo", [P, RING, UNIT_COLS], F32R)
        feat_hi = sb("feat_hi", [P, 2, BLOCKS, D], F32R)
        feat_lo = sb("feat_lo", [P, 2, BLOCKS, D], F32R)
        x_raw = sb("x_raw", [P, 2, JB, D])
        x2_raw = sb("x2_raw", [P, 2, JB, D])
        x_norm = sb("x_norm", [P, 2, JB, D])
        stats = sb("stats", [P, JB, 6])
        mean_var = sb("mean_var", [P, JB, 2])
        var_eps = sb("var_eps", [P, JB])
        std = sb("std", [P, JB])
        rstd0 = sb("rstd0", [P, JB])
        newton = sb("newton", [P, JB])
        rstd = sb("rstd", [P, 2, JB])
        mean = sb("mean", [P, 2, JB])
        w_raw = sb("w_raw", [P, 2 * LAYERS + 2, D])
        w_hi = sb("w_hi", [P, 2 * LAYERS + 2, D], F32R)
        w_lo = sb("w_lo", [P, 2 * LAYERS + 2, D], F32R)
        bias = sb("bias", [P, 2, LAYERS])
        bias_m = sb("bias_m", [P, 1])
        eps_sb = sb("eps_sb", [P, 2])
        ax_scale = sb("ax_scale", [P, 2])
        act_f = sb("act_f", [P, 2, CW])
        act_hi = sb("act_hi", [P, 2, CW], F32R)
        act_lo = sb("act_lo", [P, 2, CW], F32R)
        x_res = sb("x_res", [P, CW])
        y_sb = sb("y_sb", [P, CW])

        acc = [bank(f"acc{b}") for b in range(2)]
        hidden = [bank(f"hidden{b}") for b in range(2)]
        merged = bank("merged")

        raw_loaded = [sem(f"raw_loaded{s}") for s in range(RING)]
        x_loaded = [sem(f"x_loaded{s}") for s in range(2)]
        x2_loaded = [sem(f"x2_loaded{s}") for s in range(2)]
        params_loaded = sem("params_loaded")
        res_loaded = sem("res_loaded")
        out_stored = sem("out_stored")
        hi_made = sem("hi_made")
        lo_made = sem("lo_made")
        unit_used = sem("unit_used")
        stats_step = sem("stats_step")
        var_made = sem("var_made")
        std_made = sem("std_made")
        rstd_made = sem("rstd_made")
        norm_made = sem("norm_made")
        feat1_hi_made = sem("feat1_hi_made")
        feat2_hi_made = sem("feat2_hi_made")
        feat1_lo_made = sem("feat1_lo_made")
        feat2_lo_made = sem("feat2_lo_made")
        w_hi_made = sem("w_hi_made")
        w_lo_made = sem("w_lo_made")
        scale_made = sem("scale_made")
        first_acc_done = sem("first_acc_done")
        hidden_done = [sem(f"hidden_done{b}") for b in range(2)]
        act_hi_made = [sem(f"act_hi_made{b}") for b in range(2)]
        act_f_made = [sem(f"act_f_made{b}") for b in range(2)]
        act_lo_made = [sem(f"act_lo_made{b}") for b in range(2)]
        merged_done = sem("merged_done")
        y_made = sem("y_made")

        def f32(ap):
            return ap.bitcast(F32)

        block = ctx.enter_context(nc.Block())

        @block.sync
        def _(sp):
            def load_unit(c, u):
                if not (isinstance(c, int) and c * U + u < RING):
                    sp.wait_ge(lo_made, c * U + (u + 1 - RING))
                sp.dma_start(adj_raw[:, u % RING, :], adj_tiles[c * U + u]).then_inc(raw_loaded[u % RING], 16)

            for u in range(U):
                if u >= 2:
                    sp.wait_ge(feat2_lo_made, u - 1)
                sp.dma_start(x2_raw[:, u % 2], x2_tiles[u]).then_inc(x2_loaded[u % 2], 16)
                if u >= 2:
                    sp.wait_ge(norm_made, u - 1)
                sp.dma_start(x_raw[:, u % 2], x_tiles[u]).then_inc(x_loaded[u % 2], 16)
                load_unit(0, u)
            with sp.Fori(1, CHUNKS) as c:
                for u in range(U):
                    load_unit(c, u)

        @block.gpsimd
        def _(pool):
            loads = [
                (w_raw[:, 0:LAYERS, :], w1_t), (w_raw[:, LAYERS:2 * LAYERS, :], w2_t),
                (w_raw[:, 2 * LAYERS:, :], wm_t), (bias[:, 0, :], b1_t), (bias[:, 1, :], b2_t), (bias_m[:, :], bm_t),
                (eps_sb[:, 0:1], eps1.partition_broadcast(P)), (eps_sb[:, 1:2], eps2.partition_broadcast(P)),
            ]
            for dst, src in loads:
                pool.dma_start(dst, src).then_inc(params_loaded, 16)
            pool.dma_start(x_res[:, :], x_t[:, 0:CW]).then_inc(res_loaded, 16)

            for u in range(U):
                s = u % 2
                rows = slice(u * JB, (u + 1) * JB)
                pool.wait_ge(x2_loaded[s], 16 * (u // 2 + 1))
                pool.wait_ge(feat2_hi_made, u + 1)
                nc.gpsimd.tensor_tensor(feat_lo[:, 1, rows, :], x2_raw[:, s], f32(feat_hi[:, 1, rows, :]),
                                        ALU.subtract).then_inc(feat2_lo_made, 1)
                pool.wait_ge(x_loaded[s], 16 * (u // 2 + 1))
                pool.wait_ge(rstd_made, u + 1)
                if u >= 2:
                    pool.wait_ge(feat1_lo_made, u - 1)
                for j in range(JB):
                    last = nc.gpsimd.tensor_scalar(x_norm[:, s, j, :], x_raw[:, s, j, :], mean[:, s, j:j + 1],
                                                   rstd[:, s, j:j + 1], ALU.subtract, ALU.mult)
                last.then_inc(norm_made, 1)

            with pool.Fori(0, CHUNKS - 1) as c:
                pool.wait_ge(y_made, c + 1)
                pool.dma_start(out_t[:, bass.ds(c * CW, CW)], y_sb[:, :]).then_inc(out_stored, 16)
                pool.wait_ge(out_stored, 16 * (c + 1))
                pool.dma_start(x_res[:, :], x_t[:, bass.ds(c * CW + CW, CW)]).then_inc(res_loaded, 16)
            pool.wait_ge(y_made, CHUNKS)
            pool.dma_start(out_t[:, N - CW:N], y_sb[:, :]).then_inc(out_stored, 16)
            pool.wait_ge(out_stored, 16 * CHUNKS)

        @block.scalar
        def _(act):
            def high_of_unit(c, u):
                act.wait_ge(raw_loaded[u % RING], 16 * (c * (U // RING) + (u // RING + 1)))
                if not (isinstance(c, int) and c * U + u < RING):
                    act.wait_ge(unit_used, c * U + (u + 1 - RING))
                nc.scalar.activation(adj_hi[:, u % RING, :], adj_raw[:, u % RING, :], ACT.Copy).then_inc(hi_made, 1)

            def operand(m, k):
                for b in BRANCH_ORDER:
                    if k == 0:
                        if b == FIRST_BRANCH:
                            act.wait_ge(first_acc_done, m + 1)
                        else:
                            act.wait_ge(unit_used, m * U + U)
                        src, kw = acc[b], dict(func=ACT.Identity, scale=ax_scale[:, b:b + 1])
                    else:
                        act.wait_ge(hidden_done[b], m * LAYERS + k)
                        src, kw = hidden[b], dict(func=ACT.Relu, bias=bias[:, b, k - 1:k])
                    nc.scalar.activation(act_hi[:, b, :], src[:, :], **kw).then_inc(act_hi_made[b], 1)
                    nc.scalar.activation(act_f[:, b, :], src[:, :], **kw).then_inc(act_f_made[b], 1)

            for u in range(U):
                s = u % 2
                rows = slice(u * JB, (u + 1) * JB)
                act.wait_ge(x2_loaded[s], 16 * (u // 2 + 1))
                nc.scalar.activation(feat_hi[:, 1, rows, :], x2_raw[:, s], ACT.Copy).then_inc(feat2_hi_made, 1)
                high_of_unit(0, u)
                act.wait_ge(var_made, u + 1)
                nc.scalar.activation(std[:, :], var_eps[:, :], ACT.Sqrt).then_inc(std_made, 1)
                act.wait_ge(norm_made, u + 1)
                nc.scalar.activation(feat_hi[:, 0, rows, :], x_norm[:, s], ACT.Relu).then_inc(feat1_hi_made, 1)
                if u == 1:
                    act.wait_ge(params_loaded, 16 * 8)
                    nc.scalar.activation(w_hi[:, :, :], w_raw[:, :, :], ACT.Copy).then_inc(w_hi_made, 1)
            act.wait_ge(scale_made, 1)
            with act.Fori(1, CHUNKS) as c:
                for u in range(U):
                    high_of_unit(c, u)
                    if u in OPERAND_AFTER:
                        operand(c - 1, OPERAND_AFTER[u])
            for k in range(STEPS):
                operand(CHUNKS - 1, k)

        @block.vector
        def _(dve):
            chain = [0]

            def step(ins):
                chain[0] += 1
                ins.then_inc(stats_step, 1)
                dve.wait_ge(stats_step, chain[0])

            def low_of_unit(c, u):
                dve.wait_ge(raw_loaded[u % RING], 16 * (c * (U // RING) + (u // RING + 1)))
                dve.wait_ge(hi_made, c * U + (u + 1))
                if not (isinstance(c, int) and c * U + u < RING):
                    dve.wait_ge(unit_used, c * U + (u + 1 - RING))
                nc.vector.tensor_tensor(adj_lo[:, u % RING, :], adj_raw[:, u % RING, :], f32(adj_hi[:, u % RING, :]),
                                        ALU.subtract).then_inc(lo_made, 1)

            def low_of_operand(m, k):
                for b in BRANCH_ORDER:
                    dve.wait_ge(act_hi_made[b], m * STEPS + (k + 1))
                    dve.wait_ge(act_f_made[b], m * STEPS + (k + 1))
                    nc.vector.tensor_tensor(act_lo[:, b, :], act_f[:, b, :], f32(act_hi[:, b, :]),
                                            ALU.subtract).then_inc(act_lo_made[b], 1)

            def result(m):
                dve.wait_ge(merged_done, m + 1)
                dve.wait_ge(res_loaded, 16 * (m + 1))
                nc.vector.scalar_tensor_tensor(y_sb[:, :], merged[:, :], bias_m[:, 0:1], x_res[:, :],
                                               ALU.add, ALU.add).then_inc(y_made, 1)

            for u in range(U):
                s = u % 2
                rows = slice(u * JB, (u + 1) * JB)
                dve.wait_ge(x_loaded[s], 16 * (u // 2 + 1))
                for j in range(JB):
                    last = nc.vector.bn_stats(stats[:, j, :], x_raw[:, s, j, :])
                step(last)
                for j in range(JB):
                    last = nc.vector.bn_aggr(mean_var[:, j, :], stats[:, j, :])
                step(last)
                nc.vector.tensor_scalar(var_eps[:, :], mean_var[:, :, 1], LN_EPS, None, ALU.add).then_inc(var_made, 1)
                if u >= 2:
                    dve.wait_ge(norm_made, u - 1)
                nc.vector.tensor_copy(mean[:, s, :], mean_var[:, :, 0])
                dve.wait_ge(std_made, u + 1)
                step(nc.vector.reciprocal(rstd0[:, :], std[:, :]))
                dve.wait_ge(var_made, u + 1)
                step(nc.vector.tensor_tensor(newton[:, :], rstd0[:, :], rstd0[:, :], ALU.mult))
                step(nc.vector.tensor_tensor(newton[:, :], newton[:, :], var_eps[:, :], ALU.mult))
                step(nc.vector.tensor_scalar(newton[:, :], newton[:, :], -0.5, 1.5, ALU.mult, ALU.add))
                nc.vector.tensor_tensor(rstd[:, s, :], rstd0[:, :], newton[:, :], ALU.mult).then_inc(rstd_made, 1)
                low_of_unit(0, u)
                dve.wait_ge(norm_made, u + 1)
                dve.wait_ge(feat1_hi_made, u + 1)
                nc.vector.scalar_tensor_tensor(feat_lo[:, 0, rows, :], x_norm[:, s], 0.0, f32(feat_hi[:, 0, rows, :]),
                                               ALU.max, ALU.subtract).then_inc(feat1_lo_made, 1)
                if u == 1:
                    dve.wait_ge(params_loaded, 16 * 8)
                    nc.vector.tensor_scalar(ax_scale[:, :], eps_sb[:, :], 1.0, 1.0, ALU.add, ALU.add).then_inc(scale_made, 1)
                    dve.wait_ge(w_hi_made, 1)
                    nc.vector.tensor_tensor(w_lo[:, :, :], w_raw[:, :, :], f32(w_hi[:, :, :]),
                                            ALU.subtract).then_inc(w_lo_made, 1)
            with dve.Fori(1, CHUNKS) as c:
                for u in range(U):
                    low_of_unit(c, u)
                    if u in OPERAND_AFTER:
                        low_of_operand(c - 1, OPERAND_AFTER[u])
                result(c - 1)
            for k in range(STEPS):
                low_of_operand(CHUNKS - 1, k)
            result(CHUNKS - 1)

        @block.tensor
        def _(pe):
            def product(out, lhs_hi, lhs_lo, rhs_hi, rhs_lo, start, stop, lo_ready=None):
                nc.tensor.matmul(out, lhs_lo, rhs_hi, start=start, stop=False)
                nc.tensor.matmul(out, lhs_hi, rhs_hi, start=False, stop=False)
                if lo_ready is not None:
                    pe.wait_ge(*lo_ready)
                return nc.tensor.matmul(out, lhs_hi, rhs_lo, start=False, stop=stop)

            def aggregate(c, u):
                s = u % RING
                pe.wait_ge(hi_made, c * U + (u + 1))
                for b in BRANCH_ORDER:
                    if isinstance(c, int):
                        pe.wait_ge(feat2_hi_made if b else feat1_hi_made, u + 1)
                        pe.wait_ge(feat2_lo_made if b else feat1_lo_made, u + 1)
                    elif u == 0:
                        pe.wait_ge(act_f_made[b], (c - 1) * STEPS + 1)
                    for j in range(JB):
                        blk = u * JB + j
                        cols = slice(j * CW, (j + 1) * CW)
                        last = product(acc[b][:, :], feat_hi[:, b, blk, :], feat_lo[:, b, blk, :],
                                       adj_hi[:, s, cols], adj_lo[:, s, cols],
                                       start=(u == 0 and j == 0), stop=(u == U - 1 and j == JB - 1),
                                       lo_ready=(lo_made, c * U + (u + 1)) if j == 0 else None)
                    if u == U - 1 and b == FIRST_BRANCH:
                        last.then_inc(first_acc_done, 1)
                last.then_inc(unit_used, 1)

            def layer(m, l):
                for b in BRANCH_ORDER:
                    w = b * LAYERS + l
                    pe.wait_ge(act_hi_made[b], m * STEPS + (l + 1))
                    pe.wait_ge(act_f_made[b], m * STEPS + (l + 1))
                    product(hidden[b][:, :], w_hi[:, w, :], w_lo[:, w, :], act_hi[:, b, :], act_lo[:, b, :],
                            start=True, stop=True,
                            lo_ready=(act_lo_made[b], m * STEPS + (l + 1))).then_inc(hidden_done[b], 1)

            def merge(m):
                for b in BRANCH_ORDER:
                    w = 2 * LAYERS + b
                    pe.wait_ge(act_hi_made[b], m * STEPS + STEPS)
                    last = product(merged[:, :], w_hi[:, w, :], w_lo[:, w, :], act_hi[:, b, :], act_lo[:, b, :],
                                   start=(b == BRANCH_ORDER[0]), stop=(b == BRANCH_ORDER[1]), lo_ready=(act_lo_made[b], m * STEPS + STEPS))
                last.then_inc(merged_done, 1)

            for u in range(U):
                aggregate(0, u)
            pe.wait_ge(w_hi_made, 1)
            pe.wait_ge(w_lo_made, 1)
            with pe.Fori(1, CHUNKS) as c:
                for u in range(U):
                    aggregate(c, u)
                    if u in LAYER_AFTER:
                        layer(c - 1, LAYER_AFTER[u])
                    if u == MERGE_AFTER:
                        merge(c - 1)
            for l in range(LAYERS):
                layer(CHUNKS - 1, l)
            merge(CHUNKS - 1)


def kernel(x, adj, L0_gnn_x2, L0_gnn_eps1, L0_gnn_eps2, L0_gnn_W1, L0_gnn_b1, L0_gnn_W2, L0_gnn_b2, L0_gnn_Wm,
           L0_gnn_bm):
    import numpy as np
    import concourse.bacc as bacc
    from concourse import mybir
    from concourse.bass_utils import run_bass_kernel_spmd

    P, CW, JB = 128, 512, 4
    x, adj, x2 = np.asarray(x), np.asarray(adj), np.asarray(L0_gnn_x2)
    n, d = x.shape
    units = n // (P * JB)

    def rows(a):
        return np.ascontiguousarray(a.reshape(units, JB, P, d).transpose(0, 2, 1, 3))

    adj_tiles = adj.reshape(n // CW, CW, units, JB, P).transpose(0, 2, 4, 3, 1)
    ins = {
        "adj_tiles": adj_tiles.reshape(n // CW * units, P, JB * CW),
        "x_tiles": rows(x),
        "x2_tiles": rows(x2),
        "x_t": x.T,
        "w1_t": np.asarray(L0_gnn_W1).transpose(2, 0, 1),
        "w2_t": np.asarray(L0_gnn_W2).transpose(2, 0, 1),
        "wm_t": np.asarray(L0_gnn_Wm).reshape(d, 2, d).transpose(2, 1, 0),
        "b1_t": np.asarray(L0_gnn_b1).T,
        "b2_t": np.asarray(L0_gnn_b2).T,
        "bm_t": np.asarray(L0_gnn_bm).reshape(d, 1),
        "eps1": np.asarray(L0_gnn_eps1),
        "eps2": np.asarray(L0_gnn_eps2),
    }
    ins = {k: np.ascontiguousarray(v) for k, v in ins.items()}
    nc = bacc.Bacc("TRN2", target_bir_lowering=False, num_devices=1)
    aps = {k: nc.dram_tensor(k, v.shape, mybir.dt.from_np(v.dtype), kind="ExternalInput").ap() for k, v in ins.items()}
    out_t = nc.dram_tensor("out_t", (d, n), mybir.dt.float32, kind="ExternalOutput").ap()
    gnn_layer_kernel(nc, out_t=out_t, **aps)
    r = run_bass_kernel_spmd(nc, [ins], core_ids=[0])
    return r.results[0]["out_t"].T
```

```python
from contextlib import ExitStack

import concourse.bass as bass
from concourse import mybir


def gnn_layer_kernel(nc, adj_tiles, x_tiles, x2_tiles, x_t, w_t, bias_t, eps, out_t):
    F32 = mybir.dt.float32
    F32R = mybir.dt.float32r
    ALU = mybir.AluOpType
    ACT = mybir.ActivationFunctionType

    UNITS_ALL, P, UNIT_COLS = adj_tiles.shape
    D = x_t.shape[0]
    N = x_t.shape[1]
    CW = 512
    JB = UNIT_COLS // CW
    CHUNKS = N // CW
    U = UNITS_ALL // CHUNKS
    BLOCKS = N // P
    RING = 4
    LAYERS = 3
    STEPS = LAYERS + 1
    MATS = 2 * LAYERS + 2
    LN_EPS = 1e-5
    BRANCH_ORDER = (1, 0)
    FIRST_BRANCH = BRANCH_ORDER[0]
    assert U % RING == 0 and U == 8

    FINE_LOADS = 3
    FINE_SIGNALS = JB - 1
    X_SLOTS = 4
    WARM_UP = 8

    LAYER_AFTER = {1: 0, 3: 1, 5: 2}
    MERGE_AFTER = 6
    OPERAND_AFTER = {1: 0, 3: 1, 5: 2, 7: 3}

    with ExitStack() as ctx:
        def sb(name, shape, dt=F32):
            return ctx.enter_context(nc.sbuf_tensor(name, shape, dt))

        def bank(name):
            return ctx.enter_context(nc.psum_tensor(name, [P, CW], F32))

        def sem(name):
            return ctx.enter_context(nc.semaphore(name))

        adj_raw = sb("adj_raw", [P, RING, UNIT_COLS])
        adj_hi = sb("adj_hi", [P, RING, UNIT_COLS], F32R)
        adj_lo = sb("adj_lo", [P, RING, UNIT_COLS], F32R)
        feat_hi = sb("feat_hi", [P, 2, BLOCKS, D], F32R)
        feat_lo = sb("feat_lo", [P, 2, BLOCKS, D], F32R)
        x_rows = sb("x_rows", [P, X_SLOTS, JB, D])
        x2_rows = sb("x2_rows", [P, X_SLOTS, JB, D])
        stats = sb("stats", [P, JB, 6])
        mean_var = sb("mean_var", [P, JB, 2])
        var_eps = sb("var_eps", [P, JB])
        std = sb("std", [P, JB])
        rstd0 = sb("rstd0", [P, JB])
        newton = sb("newton", [P, JB])
        rstd = sb("rstd", [P, JB])
        shift = sb("shift", [P, JB])
        w_raw = sb("w_raw", [P, MATS, D])
        w_hi = sb("w_hi", [P, MATS, D], F32R)
        w_lo = sb("w_lo", [P, MATS, D], F32R)
        bias = sb("bias", [P, MATS - 1])
        eps_sb = sb("eps_sb", [P, 2])
        ax_scale = sb("ax_scale", [P, 2])
        root_of_zero = sb("root_of_zero", [P, 1])
        zeros = sb("zeros", [P, CW], mybir.dt.bfloat16)
        act_f = sb("act_f", [P, 2, CW])
        act_hi = sb("act_hi", [P, 2, CW], F32R)
        act_lo = sb("act_lo", [P, 2, CW], F32R)
        x_res = sb("x_res", [P, CW])
        y_sb = sb("y_sb", [P, CW])

        acc = [bank(f"acc{b}") for b in range(2)]
        hidden = [bank(f"hidden{b}") for b in range(2)]
        merged = bank("merged")

        raw_loaded = [sem(f"raw_loaded{s}") for s in range(RING)]
        fine_loaded = [sem(f"fine_loaded{s}") for s in range(FINE_LOADS * FINE_SIGNALS)]
        x_loaded = [sem(f"x_loaded{s}") for s in range(X_SLOTS)]
        x2_loaded = [sem(f"x2_loaded{s}") for s in range(X_SLOTS)]
        w_loaded = sem("w_loaded")
        bias_loaded = sem("bias_loaded")
        eps_loaded = sem("eps_loaded")
        res_loaded = sem("res_loaded")
        out_stored = sem("out_stored")
        hi_made = sem("hi_made")
        lo_made = sem("lo_made")
        fine_hi_made = sem("fine_hi_made")
        fine_lo_made = sem("fine_lo_made")
        zeros_made = sem("zeros_made")
        unit_used = sem("unit_used")
        stats_step = sem("stats_step")
        var_made = sem("var_made")
        std_made = sem("std_made")
        rstd_made = sem("rstd_made")
        feat1_hi_made = sem("feat1_hi_made")
        relu_made = sem("relu_made")
        feat2_hi_made = sem("feat2_hi_made")
        feat1_lo_made = sem("feat1_lo_made")
        feat2_lo_made = sem("feat2_lo_made")
        w_hi_made = sem("w_hi_made")
        w_lo_made = sem("w_lo_made")
        scale_made = sem("scale_made")
        first_acc_done = sem("first_acc_done")
        hidden_done = [sem(f"hidden_done{b}") for b in range(2)]
        act_hi_made = [sem(f"act_hi_made{b}") for b in range(2)]
        act_f_made = [sem(f"act_f_made{b}") for b in range(2)]
        act_lo_made = [sem(f"act_lo_made{b}") for b in range(2)]
        merged_done = sem("merged_done")
        y_made = sem("y_made")

        def f32(ap):
            return ap.bitcast(F32)

        block = ctx.enter_context(nc.Block())

        @block.sync
        def _(sp):
            def load_unit(c, u):
                if not (isinstance(c, int) and c * U + u < RING):
                    sp.wait_ge(lo_made, c * U + (u + 1 - RING))
                sp.dma_start(adj_raw[:, u % RING, :], adj_tiles[c * U + u]).then_inc(raw_loaded[u % RING], 16)

            def load_x(u):
                if u >= X_SLOTS:
                    sp.wait_ge(feat1_lo_made, u + 1 - X_SLOTS)
                sp.dma_start(x_rows[:, u % X_SLOTS], x_tiles[u]).then_inc(x_loaded[u % X_SLOTS], 16)

            for u in range(U):
                load_x(u)
                if u >= X_SLOTS:
                    sp.wait_ge(feat2_lo_made, u + 1 - X_SLOTS)
                sp.dma_start(x2_rows[:, u % X_SLOTS], x2_tiles[u]).then_inc(x2_loaded[u % X_SLOTS], 16)
                if u < FINE_LOADS:
                    for j in range(JB):
                        cols = slice(j * CW, (j + 1) * CW)
                        done = fine_loaded[u * FINE_SIGNALS + j] if j < FINE_SIGNALS else raw_loaded[u]
                        sp.dma_start(adj_raw[:, u, cols], adj_tiles[u][:, cols]).then_inc(done, 16)
                else:
                    load_unit(0, u)
                if u == U - 2:
                    sp.dma_start(w_raw[:, :, :], w_t).then_inc(w_loaded, 16)
                    sp.dma_start(bias[:, :], bias_t).then_inc(bias_loaded, 16)
                    sp.dma_start(eps_sb[:, :], eps.partition_broadcast(P)).then_inc(eps_loaded, 16)
            with sp.Fori(1, CHUNKS) as c:
                for u in range(U):
                    load_unit(c, u)

        @block.gpsimd
        def _(pool):
            for u in range(U):
                rows = slice(u * JB, (u + 1) * JB)
                pool.wait_ge(x2_loaded[u % X_SLOTS], 16 * (u // X_SLOTS + 1))
                pool.wait_ge(feat2_hi_made, u + 1)
                nc.gpsimd.tensor_tensor(feat_lo[:, 1, rows, :], x2_rows[:, u % X_SLOTS], f32(feat_hi[:, 1, rows, :]),
                                        ALU.subtract).then_inc(feat2_lo_made, 1)
                pool.wait_ge(feat1_hi_made, u + 1)
                pool.wait_ge(relu_made, u + 1)
                nc.gpsimd.tensor_tensor(feat_lo[:, 0, rows, :], x_rows[:, u % X_SLOTS], f32(feat_hi[:, 0, rows, :]),
                                        ALU.subtract).then_inc(feat1_lo_made, 1)
            pool.dma_start(x_res[:, :], x_t[:, 0:CW]).then_inc(res_loaded, 16)

            with pool.Fori(0, CHUNKS - 1) as c:
                pool.wait_ge(y_made, c + 1)
                pool.dma_start(out_t[:, bass.ds(c * CW, CW)], y_sb[:, :]).then_inc(out_stored, 16)
                pool.wait_ge(out_stored, 16 * (c + 1))
                pool.dma_start(x_res[:, :], x_t[:, bass.ds(c * CW + CW, CW)]).then_inc(res_loaded, 16)
            pool.wait_ge(y_made, CHUNKS)
            pool.dma_start(out_t[:, N - CW:N], y_sb[:, :]).then_inc(out_stored, 16)
            pool.wait_ge(out_stored, 16 * CHUNKS)

        @block.scalar
        def _(act):
            def high_of_unit(c, u):
                act.wait_ge(raw_loaded[u % RING], 16 * (c * (U // RING) + (u // RING + 1)))
                if not (isinstance(c, int) and c * U + u < RING):
                    act.wait_ge(unit_used, c * U + (u + 1 - RING))
                nc.scalar.activation(adj_hi[:, u % RING, :], adj_raw[:, u % RING, :], ACT.Copy).then_inc(hi_made, 1)

            def operand(m, k):
                for b in BRANCH_ORDER:
                    if k == 0:
                        if b == FIRST_BRANCH:
                            act.wait_ge(first_acc_done, m + 1)
                        else:
                            act.wait_ge(unit_used, m * U + U)
                        src, kw = acc[b], dict(func=ACT.Identity, scale=ax_scale[:, b:b + 1])
                    else:
                        act.wait_ge(hidden_done[b], m * LAYERS + k)
                        src, kw = hidden[b], dict(func=ACT.Relu, bias=bias[:, b * LAYERS + k - 1:b * LAYERS + k])
                    nc.scalar.activation(act_hi[:, b, :], src[:, :], **kw).then_inc(act_hi_made[b], 1)
                    nc.scalar.activation(act_f[:, b, :], src[:, :], **kw).then_inc(act_f_made[b], 1)

            def fine_high(u, j):
                slot, cols = u % RING, slice(j * CW, (j + 1) * CW)
                last = j == FINE_SIGNALS
                if u < FINE_LOADS and not last:
                    act.wait_ge(fine_loaded[u * FINE_SIGNALS + j], 16)
                else:
                    act.wait_ge(raw_loaded[slot], 16 * (u // RING + 1))
                if u >= RING:
                    act.wait_ge(unit_used, u + 1 - RING)
                nc.scalar.activation(adj_hi[:, slot, cols], adj_raw[:, slot, cols], ACT.Copy).then_inc(
                    hi_made if last else fine_hi_made, 1)

            def high_of_x2(u):
                act.wait_ge(x2_loaded[u % X_SLOTS], 16 * (u // X_SLOTS + 1))
                nc.scalar.activation(feat_hi[:, 1, u * JB:(u + 1) * JB, :], x2_rows[:, u % X_SLOTS],
                                     ACT.Copy).then_inc(feat2_hi_made, 1)

            def std_of_x(u):
                act.wait_ge(var_made, u + 1)
                nc.scalar.activation(std[:, :], var_eps[:, :], ACT.Sqrt).then_inc(std_made, 1)

            def rectify(u):
                act.wait_ge(rstd_made, u + 1)
                for j in range(JB):
                    xs = x_rows[:, u % X_SLOTS, j, :]
                    last = nc.scalar.activation(xs, xs, ACT.Relu, bias=shift[:, j:j + 1], scale=rstd[:, j:j + 1])
                last.then_inc(relu_made, 1)
                act.wait_ge(relu_made, u + 1)
                nc.scalar.activation(feat_hi[:, 0, u * JB:(u + 1) * JB, :], x_rows[:, u % X_SLOTS],
                                     ACT.Copy).then_inc(feat1_hi_made, 1)

            act.wait_ge(zeros_made, 1)
            nc.scalar.activation(root_of_zero[:, :], zeros[:, 0:1], ACT.Sqrt)
            for u in range(U):
                high_of_x2(u)
                std_of_x(u)
                for j in range(JB):
                    fine_high(u, j)
                rectify(u)
            act.wait_ge(w_loaded, 16)
            nc.scalar.activation(w_hi[:, :, :], w_raw[:, :, :], ACT.Copy).then_inc(w_hi_made, 1)
            act.wait_ge(bias_loaded, 16)
            act.wait_ge(scale_made, 1)
            with act.Fori(1, CHUNKS) as c:
                for u in range(U):
                    high_of_unit(c, u)
                    if u in OPERAND_AFTER:
                        operand(c - 1, OPERAND_AFTER[u])
            for k in range(STEPS):
                operand(CHUNKS - 1, k)

        @block.vector
        def _(dve):
            chain = [0]

            def step(ins):
                chain[0] += 1
                ins.then_inc(stats_step, 1)
                dve.wait_ge(stats_step, chain[0])

            def low_of_unit(c, u):
                dve.wait_ge(raw_loaded[u % RING], 16 * (c * (U // RING) + (u // RING + 1)))
                dve.wait_ge(hi_made, c * U + (u + 1))
                if not (isinstance(c, int) and c * U + u < RING):
                    dve.wait_ge(unit_used, c * U + (u + 1 - RING))
                nc.vector.tensor_tensor(adj_lo[:, u % RING, :], adj_raw[:, u % RING, :], f32(adj_hi[:, u % RING, :]),
                                        ALU.subtract).then_inc(lo_made, 1)

            def low_of_operand(m, k):
                for b in BRANCH_ORDER:
                    dve.wait_ge(act_hi_made[b], m * STEPS + (k + 1))
                    dve.wait_ge(act_f_made[b], m * STEPS + (k + 1))
                    nc.vector.tensor_tensor(act_lo[:, b, :], act_f[:, b, :], f32(act_hi[:, b, :]),
                                            ALU.subtract).then_inc(act_lo_made[b], 1)

            def result(m):
                dve.wait_ge(merged_done, m + 1)
                dve.wait_ge(res_loaded, 16 * (m + 1))
                nc.vector.scalar_tensor_tensor(y_sb[:, :], merged[:, :], bias[:, MATS - 2:MATS - 1], x_res[:, :],
                                               ALU.add, ALU.add).then_inc(y_made, 1)

            def variances(u):
                dve.wait_ge(x_loaded[u % X_SLOTS], 16 * (u // X_SLOTS + 1))
                for j in range(JB):
                    last = nc.vector.bn_stats(stats[:, j, :], x_rows[:, u % X_SLOTS, j, :])
                step(last)
                for j in range(JB):
                    last = nc.vector.bn_aggr(mean_var[:, j, :], stats[:, j, :])
                step(last)
                nc.vector.tensor_scalar(var_eps[:, :], mean_var[:, :, 1], LN_EPS, None, ALU.add).then_inc(var_made, 1)

            def scale_and_shift(u):
                r0, nt = rstd0[:, :], newton[:, :]
                dve.wait_ge(std_made, u + 1)
                step(nc.vector.reciprocal(r0, std[:, :]))
                step(nc.vector.tensor_tensor(nt, r0, r0, ALU.mult))
                step(nc.vector.scalar_tensor_tensor(nt, nt, -0.5, var_eps[:, :], ALU.mult, ALU.mult))
                step(nc.vector.scalar_tensor_tensor(rstd[:, :], nt, 1.5, r0, ALU.add, ALU.mult))
                nc.vector.scalar_tensor_tensor(shift[:, :], mean_var[:, :, 0], -1.0, rstd[:, :],
                                               ALU.mult, ALU.mult).then_inc(rstd_made, 1)

            def fine_low(u, j):
                slot, cols = u % RING, slice(j * CW, (j + 1) * CW)
                last = j == FINE_SIGNALS
                if u < FINE_LOADS and not last:
                    dve.wait_ge(fine_loaded[u * FINE_SIGNALS + j], 16)
                else:
                    dve.wait_ge(raw_loaded[slot], 16 * (u // RING + 1))
                if last:
                    dve.wait_ge(hi_made, u + 1)
                else:
                    dve.wait_ge(fine_hi_made, u * FINE_SIGNALS + j + 1)
                if u >= RING:
                    dve.wait_ge(unit_used, u + 1 - RING)
                nc.vector.tensor_tensor(adj_lo[:, slot, cols], adj_raw[:, slot, cols], f32(adj_hi[:, slot, cols]),
                                        ALU.subtract).then_inc(lo_made if last else fine_lo_made, 1)

            nc.vector.memset(zeros[:, :], 0.0).then_inc(zeros_made, 1)
            for u in range(U):
                variances(u)
                scale_and_shift(u)
                for j in range(JB):
                    fine_low(u, j)
            dve.wait_ge(eps_loaded, 16)
            dve.wait_ge(bias_loaded, 16)
            nc.vector.tensor_scalar(ax_scale[:, :], eps_sb[:, :], 1.0, 1.0, ALU.add, ALU.add).then_inc(scale_made, 1)
            dve.wait_ge(w_loaded, 16)
            dve.wait_ge(w_hi_made, 1)
            nc.vector.tensor_tensor(w_lo[:, :, :], w_raw[:, :, :], f32(w_hi[:, :, :]),
                                    ALU.subtract).then_inc(w_lo_made, 1)
            with dve.Fori(1, CHUNKS) as c:
                for u in range(U):
                    low_of_unit(c, u)
                    if u in OPERAND_AFTER:
                        low_of_operand(c - 1, OPERAND_AFTER[u])
                result(c - 1)
            for k in range(STEPS):
                low_of_operand(CHUNKS - 1, k)
            result(CHUNKS - 1)

        @block.tensor
        def _(pe):
            def product(out, lhs_hi, lhs_lo, rhs_hi, rhs_lo, start, stop, lo_ready):
                nc.tensor.matmul(out, lhs_hi, rhs_hi, start=start, stop=False)
                nc.tensor.matmul(out, lhs_lo, rhs_hi, start=False, stop=False)
                pe.wait_ge(*lo_ready)
                return nc.tensor.matmul(out, lhs_hi, rhs_lo, start=False, stop=stop)

            def aggregate(c, u, b):
                s = u % RING
                first_chunk = isinstance(c, int)
                fine = first_chunk and b == FIRST_BRANCH
                if first_chunk:
                    pe.wait_ge(feat2_hi_made if b else feat1_hi_made, u + 1)
                elif u == 0:
                    pe.wait_ge(act_f_made[b], (c - 1) * STEPS + 1)
                if not fine:
                    pe.wait_ge(hi_made, c * U + (u + 1))
                for j in range(JB):
                    if fine and j < FINE_SIGNALS:
                        pe.wait_ge(fine_hi_made, u * FINE_SIGNALS + j + 1)
                    elif fine:
                        pe.wait_ge(hi_made, u + 1)
                    nc.tensor.matmul(acc[b][:, :], feat_hi[:, b, u * JB + j, :], adj_hi[:, s, j * CW:(j + 1) * CW],
                                     start=(u == 0 and j == 0), stop=False)
                if first_chunk:
                    pe.wait_ge(feat2_lo_made if b else feat1_lo_made, u + 1)
                for j in range(JB):
                    nc.tensor.matmul(acc[b][:, :], feat_lo[:, b, u * JB + j, :], adj_hi[:, s, j * CW:(j + 1) * CW],
                                     start=False, stop=False)
                if not fine:
                    pe.wait_ge(lo_made, c * U + (u + 1))
                for j in range(JB):
                    if fine and j < FINE_SIGNALS:
                        pe.wait_ge(fine_lo_made, u * FINE_SIGNALS + j + 1)
                    elif fine:
                        pe.wait_ge(lo_made, u + 1)
                    last = nc.tensor.matmul(acc[b][:, :], feat_hi[:, b, u * JB + j, :],
                                            adj_lo[:, s, j * CW:(j + 1) * CW],
                                            start=False, stop=(u == U - 1 and j == JB - 1))
                if b != FIRST_BRANCH:
                    last.then_inc(unit_used, 1)
                elif u == U - 1:
                    last.then_inc(first_acc_done, 1)

            def layer(m, l):
                for b in BRANCH_ORDER:
                    w = b * LAYERS + l
                    pe.wait_ge(act_hi_made[b], m * STEPS + (l + 1))
                    pe.wait_ge(act_f_made[b], m * STEPS + (l + 1))
                    product(hidden[b][:, :], w_hi[:, w, :], w_lo[:, w, :], act_hi[:, b, :], act_lo[:, b, :],
                            start=True, stop=True,
                            lo_ready=(act_lo_made[b], m * STEPS + (l + 1))).then_inc(hidden_done[b], 1)

            def merge(m):
                for b in BRANCH_ORDER:
                    w = 2 * LAYERS + b
                    pe.wait_ge(act_hi_made[b], m * STEPS + STEPS)
                    last = product(merged[:, :], w_hi[:, w, :], w_lo[:, w, :], act_hi[:, b, :], act_lo[:, b, :],
                                   start=(b == BRANCH_ORDER[0]), stop=(b == BRANCH_ORDER[1]), lo_ready=(act_lo_made[b], m * STEPS + STEPS))
                last.then_inc(merged_done, 1)

            pe.wait_ge(zeros_made, 1)
            for _ in range(WARM_UP):
                nc.tensor.matmul(merged[:, :], zeros[:, 0:P], zeros[:, :], start=True, stop=True)
            for u in range(U):
                for b in BRANCH_ORDER:
                    aggregate(0, u, b)
            pe.wait_ge(w_hi_made, 1)
            pe.wait_ge(w_lo_made, 1)
            with pe.Fori(1, CHUNKS) as c:
                for u in range(U):
                    for b in BRANCH_ORDER:
                        aggregate(c, u, b)
                    if u in LAYER_AFTER:
                        layer(c - 1, LAYER_AFTER[u])
                    if u == MERGE_AFTER:
                        merge(c - 1)
            for l in range(LAYERS):
                layer(CHUNKS - 1, l)
            merge(CHUNKS - 1)


def kernel(x, adj, L0_gnn_x2, L0_gnn_eps1, L0_gnn_eps2, L0_gnn_W1, L0_gnn_b1, L0_gnn_W2, L0_gnn_b2, L0_gnn_Wm,
           L0_gnn_bm):
    import numpy as np
    import concourse.bacc as bacc
    from concourse import mybir
    from concourse.bass_utils import run_bass_kernel_spmd

    P, CW, JB = 128, 512, 4
    x, adj, x2 = np.asarray(x), np.asarray(adj), np.asarray(L0_gnn_x2)
    n, d = x.shape
    units = n // (P * JB)

    def rows(a):
        return np.ascontiguousarray(a.reshape(units, JB, P, d).transpose(0, 2, 1, 3))

    adj_tiles = adj.reshape(n // CW, CW, units, JB, P).transpose(0, 2, 4, 3, 1)
    ins = {
        "adj_tiles": adj_tiles.reshape(n // CW * units, P, JB * CW),
        "x_tiles": rows(x),
        "x2_tiles": rows(x2),
        "x_t": x.T,
        "w_t": np.concatenate([np.asarray(L0_gnn_W1).transpose(2, 0, 1), np.asarray(L0_gnn_W2).transpose(2, 0, 1),
                               np.asarray(L0_gnn_Wm).reshape(d, 2, d).transpose(2, 1, 0)], axis=1),
        "bias_t": np.concatenate([np.asarray(L0_gnn_b1), np.asarray(L0_gnn_b2),
                                  np.asarray(L0_gnn_bm).reshape(1, d)]).T,
        "eps": np.concatenate([np.asarray(L0_gnn_eps1), np.asarray(L0_gnn_eps2)]),
    }
    ins = {k: np.ascontiguousarray(v) for k, v in ins.items()}
    nc = bacc.Bacc("TRN2", target_bir_lowering=False, num_devices=1)
    aps = {k: nc.dram_tensor(k, v.shape, mybir.dt.from_np(v.dtype), kind="ExternalInput").ap() for k, v in ins.items()}
    out_t = nc.dram_tensor("out_t", (d, n), mybir.dt.float32, kind="ExternalOutput").ap()
    gnn_layer_kernel(nc, out_t=out_t, **aps)
    r = run_bass_kernel_spmd(nc, [ins], core_ids=[0])
    return r.results[0]["out_t"].T
```

```python
from contextlib import ExitStack

import concourse.bass as bass
from concourse import mybir


def gnn_layer_kernel(nc, adj_tiles, x_tiles, x2_tiles, x_t, w_t, bias_t, eps, out_t):
    F32 = mybir.dt.float32
    F32R = mybir.dt.float32r
    ALU = mybir.AluOpType
    ACT = mybir.ActivationFunctionType

    UNITS_ALL, P, UNIT_COLS = adj_tiles.shape
    D = x_t.shape[0]
    N = x_t.shape[1]
    CW = 512
    JB = UNIT_COLS // CW
    CHUNKS = N // CW
    U = UNITS_ALL // CHUNKS
    BLOCKS = N // P
    RING = 4
    LAYERS = 3
    STEPS = LAYERS + 1
    MATS = 2 * LAYERS + 2
    LN_EPS = 1e-5
    BRANCH_ORDER = (1, 0)
    FIRST_BRANCH = BRANCH_ORDER[0]
    assert U % RING == 0 and U == 8

    FINE_LOADS = 3
    FINE_SIGNALS = JB - 1
    X_SLOTS = 4
    WARM_UP = 12

    LAYER_AFTER = {1: 0, 3: 1, 5: 2}
    MERGE_AFTER = 6
    OPERAND_AFTER = {1: 0, 3: 1, 5: 2, 7: 3}

    with ExitStack() as ctx:
        def sb(name, shape, dt=F32):
            return ctx.enter_context(nc.sbuf_tensor(name, shape, dt))

        def bank(name):
            return ctx.enter_context(nc.psum_tensor(name, [P, CW], F32))

        def sem(name):
            return ctx.enter_context(nc.semaphore(name))

        adj_raw = sb("adj_raw", [P, RING, UNIT_COLS])
        adj_hi = sb("adj_hi", [P, RING, UNIT_COLS], F32R)
        adj_lo = sb("adj_lo", [P, RING, UNIT_COLS], F32R)
        feat_hi = sb("feat_hi", [P, 2, BLOCKS, D], F32R)
        feat_lo = sb("feat_lo", [P, 2, BLOCKS, D], F32R)
        x_rows = sb("x_rows", [P, X_SLOTS, JB, D])
        x2_rows = sb("x2_rows", [P, X_SLOTS, JB, D])
        stats = sb("stats", [P, JB, 6])
        mean_var = sb("mean_var", [P, JB, 2])
        var_eps = sb("var_eps", [P, JB])
        std = sb("std", [P, JB])
        rstd0 = sb("rstd0", [P, JB])
        newton = sb("newton", [P, JB])
        rstd = sb("rstd", [P, JB])
        shift = sb("shift", [P, JB])
        w_raw = sb("w_raw", [P, MATS, D])
        w_hi = sb("w_hi", [P, MATS, D], F32R)
        w_lo = sb("w_lo", [P, MATS, D], F32R)
        bias = sb("bias", [P, MATS - 1])
        eps_sb = sb("eps_sb", [P, 2])
        ax_scale = sb("ax_scale", [P, 2])
        root_of_zero = sb("root_of_zero", [P, 1])
        zeros = sb("zeros", [P, CW], mybir.dt.bfloat16)
        act_f = sb("act_f", [P, 2, CW])
        act_hi = sb("act_hi", [P, 2, CW], F32R)
        act_lo = sb("act_lo", [P, 2, CW], F32R)
        x_res = sb("x_res", [P, CW])
        y_sb = sb("y_sb", [P, CW])

        acc = [bank(f"acc{b}") for b in range(2)]
        hidden = [bank(f"hidden{b}") for b in range(2)]
        merged = bank("merged")

        raw_loaded = [sem(f"raw_loaded{s}") for s in range(RING)]
        fine_loaded = [sem(f"fine_loaded{s}") for s in range(FINE_LOADS * FINE_SIGNALS)]
        x_loaded = [sem(f"x_loaded{s}") for s in range(X_SLOTS)]
        x2_loaded = [sem(f"x2_loaded{s}") for s in range(X_SLOTS)]
        w_loaded = sem("w_loaded")
        bias_loaded = sem("bias_loaded")
        eps_loaded = sem("eps_loaded")
        res_loaded = sem("res_loaded")
        out_stored = sem("out_stored")
        last_stored = sem("last_stored")
        hi_made = sem("hi_made")
        lo_made = sem("lo_made")
        fine_hi_made = sem("fine_hi_made")
        fine_lo_made = sem("fine_lo_made")
        zeros_made = sem("zeros_made")
        unit_used = sem("unit_used")
        stats_step = sem("stats_step")
        var_made = sem("var_made")
        std_made = sem("std_made")
        rstd_made = sem("rstd_made")
        feat1_hi_made = sem("feat1_hi_made")
        relu_made = sem("relu_made")
        feat2_hi_made = sem("feat2_hi_made")
        feat1_lo_made = sem("feat1_lo_made")
        feat2_lo_made = sem("feat2_lo_made")
        w_hi_made = sem("w_hi_made")
        w_lo_made = sem("w_lo_made")
        scale_made = sem("scale_made")
        first_acc_done = sem("first_acc_done")
        hidden_done = [sem(f"hidden_done{b}") for b in range(2)]
        act_hi_made = [sem(f"act_hi_made{b}") for b in range(2)]
        act_f_made = [sem(f"act_f_made{b}") for b in range(2)]
        act_lo_made = [sem(f"act_lo_made{b}") for b in range(2)]
        merged_done = sem("merged_done")
        y_made = sem("y_made")

        def f32(ap):
            return ap.bitcast(F32)

        block = ctx.enter_context(nc.Block())

        @block.sync
        def _(sp):
            def load_unit(c, u):
                if not (isinstance(c, int) and c * U + u < RING):
                    sp.wait_ge(lo_made, c * U + (u + 1 - RING))
                sp.dma_start(adj_raw[:, u % RING, :], adj_tiles[c * U + u]).then_inc(raw_loaded[u % RING], 16)

            def load_x(u):
                if u >= X_SLOTS:
                    sp.wait_ge(feat1_lo_made, u + 1 - X_SLOTS)
                sp.dma_start(x_rows[:, u % X_SLOTS], x_tiles[u]).then_inc(x_loaded[u % X_SLOTS], 16)

            for u in range(U):
                load_x(u)
                if u >= X_SLOTS:
                    sp.wait_ge(feat2_lo_made, u + 1 - X_SLOTS)
                sp.dma_start(x2_rows[:, u % X_SLOTS], x2_tiles[u]).then_inc(x2_loaded[u % X_SLOTS], 16)
                if u < FINE_LOADS:
                    for j in range(JB):
                        cols = slice(j * CW, (j + 1) * CW)
                        done = fine_loaded[u * FINE_SIGNALS + j] if j < FINE_SIGNALS else raw_loaded[u]
                        sp.dma_start(adj_raw[:, u, cols], adj_tiles[u][:, cols]).then_inc(done, 16)
                else:
                    load_unit(0, u)
                if u == U - 2:
                    sp.dma_start(w_raw[:, :, :], w_t).then_inc(w_loaded, 16)
                    sp.dma_start(bias[:, :], bias_t).then_inc(bias_loaded, 16)
                    sp.dma_start(eps_sb[:, :], eps.partition_broadcast(P)).then_inc(eps_loaded, 16)
            with sp.Fori(1, CHUNKS) as c:
                for u in range(U):
                    load_unit(c, u)
            sp.wait_ge(y_made, CHUNKS)
            sp.dma_start(out_t[:, N - CW:N], y_sb[:, :]).then_inc(last_stored, 16)
            sp.wait_ge(last_stored, 16)

        @block.gpsimd
        def _(pool):
            for u in range(U):
                rows = slice(u * JB, (u + 1) * JB)
                pool.wait_ge(x2_loaded[u % X_SLOTS], 16 * (u // X_SLOTS + 1))
                pool.wait_ge(feat2_hi_made, u + 1)
                nc.gpsimd.tensor_tensor(feat_lo[:, 1, rows, :], x2_rows[:, u % X_SLOTS], f32(feat_hi[:, 1, rows, :]),
                                        ALU.subtract).then_inc(feat2_lo_made, 1)
                pool.wait_ge(feat1_hi_made, u + 1)
                pool.wait_ge(relu_made, u + 1)
                nc.gpsimd.tensor_tensor(feat_lo[:, 0, rows, :], x_rows[:, u % X_SLOTS], f32(feat_hi[:, 0, rows, :]),
                                        ALU.subtract).then_inc(feat1_lo_made, 1)
            pool.wait_ge(w_loaded, 16)
            nc.gpsimd.tensor_copy(w_hi[:, :, :], w_raw[:, :, :]).then_inc(w_hi_made, 1)
            pool.wait_ge(w_hi_made, 1)
            nc.gpsimd.tensor_tensor(w_lo[:, :, :], w_raw[:, :, :], f32(w_hi[:, :, :]),
                                    ALU.subtract).then_inc(w_lo_made, 1)
            pool.dma_start(x_res[:, :], x_t[:, 0:CW]).then_inc(res_loaded, 16)

            with pool.Fori(0, CHUNKS - 1) as c:
                pool.wait_ge(y_made, c + 1)
                pool.dma_start(out_t[:, bass.ds(c * CW, CW)], y_sb[:, :]).then_inc(out_stored, 16)
                pool.wait_ge(out_stored, 16 * (c + 1))
                pool.dma_start(x_res[:, :], x_t[:, bass.ds(c * CW + CW, CW)]).then_inc(res_loaded, 16)
            pool.wait_ge(out_stored, 16 * (CHUNKS - 1))

        @block.scalar
        def _(act):
            def high_of_unit(c, u):
                act.wait_ge(raw_loaded[u % RING], 16 * (c * (U // RING) + (u // RING + 1)))
                if not (isinstance(c, int) and c * U + u < RING):
                    act.wait_ge(unit_used, c * U + (u + 1 - RING))
                nc.scalar.activation(adj_hi[:, u % RING, :], adj_raw[:, u % RING, :], ACT.Copy).then_inc(hi_made, 1)

            def source(m, k, b):
                if k > 0:
                    act.wait_ge(hidden_done[b], m * LAYERS + k)
                    return hidden[b], dict(func=ACT.Relu, bias=bias[:, b * LAYERS + k - 1:b * LAYERS + k])
                if b == FIRST_BRANCH:
                    act.wait_ge(first_acc_done, m + 1)
                else:
                    act.wait_ge(unit_used, m * U + U)
                return acc[b], dict(func=ACT.Identity, scale=ax_scale[:, b:b + 1])

            def operand(m, k):
                for b in BRANCH_ORDER:
                    src, how = source(m, k, b)
                    nc.scalar.activation(act_hi[:, b, :], src[:, :], **how).then_inc(act_hi_made[b], 1)
                    nc.scalar.activation(act_f[:, b, :], src[:, :], **how).then_inc(act_f_made[b], 1)

            def last_operand(k):
                m = CHUNKS - 1
                for b in BRANCH_ORDER:
                    src, how = source(m, k, b)
                    nc.scalar.activation(act_f[:, b, :], src[:, :], **how).then_inc(act_f_made[b], 1)
                act.wait_ge(act_f_made[b], m * STEPS + (k + 1))
                nc.scalar.activation(act_hi[:, b, :], act_f[:, b, :], ACT.Copy).then_inc(act_hi_made[b], 1)

            def fine_high(u, j):
                slot, cols = u % RING, slice(j * CW, (j + 1) * CW)
                last = j == FINE_SIGNALS
                if u < FINE_LOADS and not last:
                    act.wait_ge(fine_loaded[u * FINE_SIGNALS + j], 16)
                else:
                    act.wait_ge(raw_loaded[slot], 16 * (u // RING + 1))
                if u >= RING:
                    act.wait_ge(unit_used, u + 1 - RING)
                nc.scalar.activation(adj_hi[:, slot, cols], adj_raw[:, slot, cols], ACT.Copy).then_inc(
                    hi_made if last else fine_hi_made, 1)

            def high_of_x2(u):
                act.wait_ge(x2_loaded[u % X_SLOTS], 16 * (u // X_SLOTS + 1))
                nc.scalar.activation(feat_hi[:, 1, u * JB:(u + 1) * JB, :], x2_rows[:, u % X_SLOTS],
                                     ACT.Copy).then_inc(feat2_hi_made, 1)

            def std_of_x(u):
                act.wait_ge(var_made, u + 1)
                nc.scalar.activation(std[:, :], var_eps[:, :], ACT.Sqrt).then_inc(std_made, 1)

            def rectify(u):
                act.wait_ge(rstd_made, u + 1)
                for j in range(JB):
                    xs = x_rows[:, u % X_SLOTS, j, :]
                    last = nc.scalar.activation(xs, xs, ACT.Relu, bias=shift[:, j:j + 1], scale=rstd[:, j:j + 1])
                last.then_inc(relu_made, 1)
                act.wait_ge(relu_made, u + 1)
                nc.scalar.activation(feat_hi[:, 0, u * JB:(u + 1) * JB, :], x_rows[:, u % X_SLOTS],
                                     ACT.Copy).then_inc(feat1_hi_made, 1)

            act.wait_ge(zeros_made, 1)
            nc.scalar.activation(root_of_zero[:, :], zeros[:, 0:1], ACT.Sqrt)
            for u in range(U):
                high_of_x2(u)
                std_of_x(u)
                for j in range(JB):
                    fine_high(u, j)
                rectify(u)
            act.wait_ge(bias_loaded, 16)
            act.wait_ge(scale_made, 1)
            with act.Fori(1, CHUNKS) as c:
                for u in range(U):
                    high_of_unit(c, u)
                    if u in OPERAND_AFTER:
                        operand(c - 1, OPERAND_AFTER[u])
            for k in range(STEPS):
                last_operand(k)

        @block.vector
        def _(dve):
            chain = [0]

            def step(ins):
                chain[0] += 1
                ins.then_inc(stats_step, 1)
                dve.wait_ge(stats_step, chain[0])

            def low_of_unit(c, u):
                dve.wait_ge(raw_loaded[u % RING], 16 * (c * (U // RING) + (u // RING + 1)))
                dve.wait_ge(hi_made, c * U + (u + 1))
                if not (isinstance(c, int) and c * U + u < RING):
                    dve.wait_ge(unit_used, c * U + (u + 1 - RING))
                nc.vector.tensor_tensor(adj_lo[:, u % RING, :], adj_raw[:, u % RING, :], f32(adj_hi[:, u % RING, :]),
                                        ALU.subtract).then_inc(lo_made, 1)

            def low_of_operand(m, k):
                for b in BRANCH_ORDER:
                    dve.wait_ge(act_hi_made[b], m * STEPS + (k + 1))
                    dve.wait_ge(act_f_made[b], m * STEPS + (k + 1))
                    nc.vector.tensor_tensor(act_lo[:, b, :], act_f[:, b, :], f32(act_hi[:, b, :]),
                                            ALU.subtract).then_inc(act_lo_made[b], 1)

            def result(m):
                dve.wait_ge(merged_done, m + 1)
                dve.wait_ge(res_loaded, 16 * (m + 1))
                nc.vector.scalar_tensor_tensor(y_sb[:, :], merged[:, :], bias[:, MATS - 2:MATS - 1], x_res[:, :],
                                               ALU.add, ALU.add).then_inc(y_made, 1)

            def variances(u):
                dve.wait_ge(x_loaded[u % X_SLOTS], 16 * (u // X_SLOTS + 1))
                for j in range(JB):
                    last = nc.vector.bn_stats(stats[:, j, :], x_rows[:, u % X_SLOTS, j, :])
                step(last)
                for j in range(JB):
                    last = nc.vector.bn_aggr(mean_var[:, j, :], stats[:, j, :])
                step(last)
                nc.vector.tensor_scalar(var_eps[:, :], mean_var[:, :, 1], LN_EPS, None, ALU.add).then_inc(var_made, 1)

            def scale_and_shift(u):
                r0, nt = rstd0[:, :], newton[:, :]
                dve.wait_ge(std_made, u + 1)
                step(nc.vector.reciprocal(r0, std[:, :]))
                step(nc.vector.tensor_tensor(nt, r0, r0, ALU.mult))
                step(nc.vector.scalar_tensor_tensor(nt, nt, -0.5, var_eps[:, :], ALU.mult, ALU.mult))
                step(nc.vector.scalar_tensor_tensor(rstd[:, :], nt, 1.5, r0, ALU.add, ALU.mult))
                nc.vector.scalar_tensor_tensor(shift[:, :], mean_var[:, :, 0], -1.0, rstd[:, :],
                                               ALU.mult, ALU.mult).then_inc(rstd_made, 1)

            def fine_low(u, j):
                slot, cols = u % RING, slice(j * CW, (j + 1) * CW)
                last = j == FINE_SIGNALS
                if u < FINE_LOADS and not last:
                    dve.wait_ge(fine_loaded[u * FINE_SIGNALS + j], 16)
                else:
                    dve.wait_ge(raw_loaded[slot], 16 * (u // RING + 1))
                if last:
                    dve.wait_ge(hi_made, u + 1)
                else:
                    dve.wait_ge(fine_hi_made, u * FINE_SIGNALS + j + 1)
                if u >= RING:
                    dve.wait_ge(unit_used, u + 1 - RING)
                nc.vector.tensor_tensor(adj_lo[:, slot, cols], adj_raw[:, slot, cols], f32(adj_hi[:, slot, cols]),
                                        ALU.subtract).then_inc(lo_made if last else fine_lo_made, 1)

            nc.vector.memset(zeros[:, :], 0.0).then_inc(zeros_made, 1)
            for u in range(U):
                variances(u)
                scale_and_shift(u)
                for j in range(JB):
                    fine_low(u, j)
            dve.wait_ge(eps_loaded, 16)
            dve.wait_ge(bias_loaded, 16)
            nc.vector.tensor_scalar(ax_scale[:, :], eps_sb[:, :], 1.0, 1.0, ALU.add, ALU.add).then_inc(scale_made, 1)
            with dve.Fori(1, CHUNKS) as c:
                for u in range(U):
                    low_of_unit(c, u)
                    if u in OPERAND_AFTER:
                        low_of_operand(c - 1, OPERAND_AFTER[u])
                result(c - 1)
            for k in range(STEPS):
                n = (CHUNKS - 1) * STEPS + (k + 1)
                dve.wait_ge(act_f_made[FIRST_BRANCH], n)
                nc.vector.tensor_copy(act_hi[:, FIRST_BRANCH, :], act_f[:, FIRST_BRANCH, :]).then_inc(
                    act_hi_made[FIRST_BRANCH], 1)
                low_of_operand(CHUNKS - 1, k)
            result(CHUNKS - 1)

        @block.tensor
        def _(pe):
            def product(out, lhs_hi, lhs_lo, rhs_hi, rhs_lo, start, stop, lo_ready):
                nc.tensor.matmul(out, lhs_lo, rhs_hi, start=start, stop=False)
                nc.tensor.matmul(out, lhs_hi, rhs_hi, start=False, stop=False)
                if lo_ready is not None:
                    pe.wait_ge(*lo_ready)
                return nc.tensor.matmul(out, lhs_hi, rhs_lo, start=False, stop=stop)

            def columns(u, j):
                return u % RING, slice(j * CW, (j + 1) * CW)

            def first_aggregate(u, b):
                fine = b == FIRST_BRANCH
                pe.wait_ge(feat2_hi_made if b else feat1_hi_made, u + 1)
                if not fine:
                    pe.wait_ge(hi_made, u + 1)
                for j in range(JB):
                    if fine and j < FINE_SIGNALS:
                        pe.wait_ge(fine_hi_made, u * FINE_SIGNALS + j + 1)
                    elif fine:
                        pe.wait_ge(hi_made, u + 1)
                    s, cols = columns(u, j)
                    nc.tensor.matmul(acc[b][:, :], feat_hi[:, b, u * JB + j, :], adj_hi[:, s, cols],
                                     start=(u == 0 and j == 0), stop=False)
                pe.wait_ge(feat2_lo_made if b else feat1_lo_made, u + 1)
                for j in range(JB):
                    s, cols = columns(u, j)
                    nc.tensor.matmul(acc[b][:, :], feat_lo[:, b, u * JB + j, :], adj_hi[:, s, cols],
                                     start=False, stop=False)
                if not fine:
                    pe.wait_ge(lo_made, u + 1)
                for j in range(JB):
                    if fine and j < FINE_SIGNALS:
                        pe.wait_ge(fine_lo_made, u * FINE_SIGNALS + j + 1)
                    elif fine:
                        pe.wait_ge(lo_made, u + 1)
                    s, cols = columns(u, j)
                    last = nc.tensor.matmul(acc[b][:, :], feat_hi[:, b, u * JB + j, :], adj_lo[:, s, cols],
                                            start=False, stop=(u == U - 1 and j == JB - 1))
                signal(u, b, last)

            def aggregate(c, u, b):
                if u == 0:
                    pe.wait_ge(act_f_made[b], (c - 1) * STEPS + 1)
                pe.wait_ge(hi_made, c * U + (u + 1))
                for j in range(JB):
                    s, cols = columns(u, j)
                    last = product(acc[b][:, :], feat_hi[:, b, u * JB + j, :], feat_lo[:, b, u * JB + j, :],
                                   adj_hi[:, s, cols], adj_lo[:, s, cols],
                                   start=(u == 0 and j == 0), stop=(u == U - 1 and j == JB - 1),
                                   lo_ready=(lo_made, c * U + (u + 1)) if j == 0 else None)
                signal(u, b, last)

            def signal(u, b, last):
                if b != FIRST_BRANCH:
                    last.then_inc(unit_used, 1)
                elif u == U - 1:
                    last.then_inc(first_acc_done, 1)

            def layer(m, l):
                if l == 0:
                    pe.wait_ge(w_hi_made, 1)
                    pe.wait_ge(w_lo_made, 1)
                for b in BRANCH_ORDER:
                    w = b * LAYERS + l
                    pe.wait_ge(act_hi_made[b], m * STEPS + (l + 1))
                    pe.wait_ge(act_f_made[b], m * STEPS + (l + 1))
                    product(hidden[b][:, :], w_hi[:, w, :], w_lo[:, w, :], act_hi[:, b, :], act_lo[:, b, :],
                            start=True, stop=True,
                            lo_ready=(act_lo_made[b], m * STEPS + (l + 1))).then_inc(hidden_done[b], 1)

            def merge(m):
                for b in BRANCH_ORDER:
                    w = 2 * LAYERS + b
                    pe.wait_ge(act_hi_made[b], m * STEPS + STEPS)
                    last = product(merged[:, :], w_hi[:, w, :], w_lo[:, w, :], act_hi[:, b, :], act_lo[:, b, :],
                                   start=(b == BRANCH_ORDER[0]), stop=(b == BRANCH_ORDER[1]), lo_ready=(act_lo_made[b], m * STEPS + STEPS))
                last.then_inc(merged_done, 1)

            pe.wait_ge(zeros_made, 1)
            for _ in range(WARM_UP):
                nc.tensor.matmul(merged[:, :], zeros[:, 0:P], zeros[:, :], start=True, stop=True)
            for u in range(U):
                for b in BRANCH_ORDER:
                    first_aggregate(u, b)
            with pe.Fori(1, CHUNKS) as c:
                for u in range(U):
                    for b in BRANCH_ORDER:
                        aggregate(c, u, b)
                    if u in LAYER_AFTER:
                        layer(c - 1, LAYER_AFTER[u])
                    if u == MERGE_AFTER:
                        merge(c - 1)
            for l in range(LAYERS):
                layer(CHUNKS - 1, l)
            merge(CHUNKS - 1)


def kernel(x, adj, L0_gnn_x2, L0_gnn_eps1, L0_gnn_eps2, L0_gnn_W1, L0_gnn_b1, L0_gnn_W2, L0_gnn_b2, L0_gnn_Wm,
           L0_gnn_bm):
    import numpy as np
    import concourse.bacc as bacc
    from concourse import mybir
    from concourse.bass_utils import run_bass_kernel_spmd

    P, CW, JB = 128, 512, 4
    x, adj, x2 = np.asarray(x), np.asarray(adj), np.asarray(L0_gnn_x2)
    n, d = x.shape
    units = n // (P * JB)

    def rows(a):
        return np.ascontiguousarray(a.reshape(units, JB, P, d).transpose(0, 2, 1, 3))

    adj_tiles = adj.reshape(n // CW, CW, units, JB, P).transpose(0, 2, 4, 3, 1)
    ins = {
        "adj_tiles": adj_tiles.reshape(n // CW * units, P, JB * CW),
        "x_tiles": rows(x),
        "x2_tiles": rows(x2),
        "x_t": x.T,
        "w_t": np.concatenate([np.asarray(L0_gnn_W1).transpose(2, 0, 1), np.asarray(L0_gnn_W2).transpose(2, 0, 1),
                               np.asarray(L0_gnn_Wm).reshape(d, 2, d).transpose(2, 1, 0)], axis=1),
        "bias_t": np.concatenate([np.asarray(L0_gnn_b1), np.asarray(L0_gnn_b2),
                                  np.asarray(L0_gnn_bm).reshape(1, d)]).T,
        "eps": np.concatenate([np.asarray(L0_gnn_eps1), np.asarray(L0_gnn_eps2)]),
    }
    ins = {k: np.ascontiguousarray(v) for k, v in ins.items()}
    nc = bacc.Bacc("TRN2", target_bir_lowering=False, num_devices=1)
    aps = {k: nc.dram_tensor(k, v.shape, mybir.dt.from_np(v.dtype), kind="ExternalInput").ap() for k, v in ins.items()}
    out_t = nc.dram_tensor("out_t", (d, n), mybir.dt.float32, kind="ExternalOutput").ap()
    gnn_layer_kernel(nc, out_t=out_t, **aps)
    r = run_bass_kernel_spmd(nc, [ins], core_ids=[0])
    return r.results[0]["out_t"].T
```
